# Optimizing a Trainium2 kernel written in Bass

```python
import numpy as np
import jax
import jax.numpy as jnp

def _softmax(x, axis=-1):
    return jax.nn.softmax(x, axis=axis)

def _gelu(x):
    return jax.nn.gelu(x, approximate=True)

def _silu(x):
    return jax.nn.silu(x)

def _sigmoid(x):
    return jax.nn.sigmoid(x)

def _layernorm(x, axis=-1, eps=1e-05):
    m = jnp.mean(x, axis=axis, keepdims=True)
    v = jnp.var(x, axis=axis, keepdims=True)
    return (x - m) / jnp.sqrt(v + eps)

def _scatter_add(tgt, idx, src, axis=0):
    return tgt.at[idx].add(src)

def _segment_sum(src, seg, n):
    return jax.ops.segment_sum(src, seg, n)
kernel_name = 'mk_seq_postln_d2_jaxref_r4_24408a'

def setup_inputs(seed: int=0):
    np.random.seed(seed)
    _w = jnp.asarray

    def _L0_attn_setup():
        import jax, jax.numpy as jnp
        import numpy as np
        DIM = 512
        HEADS = 16
        B = 4
        T = 512
        CHUNK = 128

        def _slopes(h):
            start = 2.0 ** (-2.0 ** (-(np.log2(h) - 3)))
            return np.array([start ** (i + 1) for i in range(h)], dtype=np.float32)

        def _lrpe(x, theta, offset=0):
            n = x.shape[-2]
            index = (jnp.arange(n, dtype=x.dtype) + offset).reshape(1, n, 1)
            th = theta * index
            return jnp.concatenate([x * jnp.cos(th), x * jnp.sin(th)], axis=-1)

        def _lightning_attn(q, k, v, slopes, chunk=CHUNK):
            b, h, Tn, dk = q.shape
            dv = v.shape[-1]
            nc = Tn // chunk
            s = slopes.reshape(h, 1, 1)
            idx = jnp.arange(chunk, dtype=q.dtype)
            diff = idx[:, None] - idx[None, :]
            diag_decay = jnp.where(diff >= 0, jnp.exp(-s * diff), 0.0)
            q_decay = jnp.exp(-s * (idx + 1.0)[None, :, None])
            k_decay = jnp.exp(-s * (chunk - 1.0 - idx)[None, :, None])
            block_decay = jnp.exp(-slopes * chunk).reshape(1, h, 1, 1)
            qc = q.reshape(b, h, nc, chunk, dk).transpose(2, 0, 1, 3, 4)
            kc = k.reshape(b, h, nc, chunk, dk).transpose(2, 0, 1, 3, 4)
            vc = v.reshape(b, h, nc, chunk, dv).transpose(2, 0, 1, 3, 4)

            def step(state, inp):
                qi, ki, vi = inp
                scores = jnp.einsum('bhid,bhjd->bhij', qi, ki) * diag_decay
                o = jnp.einsum('bhij,bhjv->bhiv', scores, vi) + jnp.einsum('bhid,bhdv->bhiv', qi * q_decay, state)
                state = block_decay * state + jnp.einsum('bhjd,bhjv->bhdv', ki * k_decay, vi)
                return (state, o)
            state0 = jnp.zeros((b, h, dk, dv), q.dtype)
            _, o = jax.lax.scan(step, state0, (qc, kc, vc))
            return o.transpose(1, 2, 0, 3, 4).reshape(b, h, Tn, dv)
        key = jax.random.key(seed)
        k1, k2, k3 = jax.random.split(key, 3)
        x = jax.random.normal(k1, (B, T, DIM), jnp.float32)
        w_qkv = jax.random.normal(k2, (3 * DIM, DIM), jnp.float32) * 0.02
        w_proj = jax.random.normal(k3, (DIM, DIM), jnp.float32) * 0.02
        e = DIM // HEADS
        theta = (10000.0 ** (-2.0 / DIM * jnp.arange(DIM, dtype=jnp.float32))).reshape(HEADS, 1, e)
        return {'x': x, 'w_qkv': w_qkv, 'w_proj': w_proj, 'theta': theta}
    _L0_attn_in = _L0_attn_setup()

    def _L0_ffn_setup():
        import jax, jax.numpy as jnp
        import numpy as np
        HIDDEN = 512
        INTER = 2048
        B, S = (4, 256)

        def _qmatmul(x, w_int8, scale):
            y = jnp.einsum('bsh,ho->bso', x, w_int8.astype(x.dtype))
            return y * scale
        key = jax.random.key(seed)
        ks = jax.random.split(key, 7)
        x = jax.random.normal(ks[0], (B, S, HIDDEN), dtype=jnp.float32)
        w_gate = jax.random.randint(ks[1], (HIDDEN, INTER), -128, 128, dtype=jnp.int32).astype(jnp.int8)
        w_up = jax.random.randint(ks[2], (HIDDEN, INTER), -128, 128, dtype=jnp.int32).astype(jnp.int8)
        w_down = jax.random.randint(ks[3], (INTER, HIDDEN), -128, 128, dtype=jnp.int32).astype(jnp.int8)
        s_gate = jax.random.uniform(ks[4], (INTER,), dtype=jnp.float32) * 0.02 + 0.001
        s_up = jax.random.uniform(ks[5], (INTER,), dtype=jnp.float32) * 0.02 + 0.001
        s_down = jax.random.uniform(ks[6], (HIDDEN,), dtype=jnp.float32) * 0.02 + 0.001
        return {'x': x, 'w_gate': w_gate, 'w_up': w_up, 'w_down': w_down, 's_gate': s_gate, 's_up': s_up, 's_down': s_down}
    _L0_ffn_in = _L0_ffn_setup()

    def _L1_attn_setup():
        import jax, jax.numpy as jnp
        import numpy as np
        DIM = 512
        key = jax.random.key(seed)
        ks = jax.random.split(key, 9)
        scale = 1.0 / np.sqrt(DIM)
        x = jax.random.normal(ks[0], (4, 1024, DIM), dtype=jnp.float32)

        def lin(kw, kb):
            W = jax.random.uniform(kw, (DIM, DIM), jnp.float32, -scale, scale)
            b = jax.random.uniform(kb, (DIM,), jnp.float32, -scale, scale)
            return (W, b)
        Wq, bq = lin(ks[1], ks[2])
        Wk, bk = lin(ks[3], ks[4])
        Wv, bv = lin(ks[5], ks[6])
        Wg, bg = lin(ks[7], ks[8])
        return {'x': x, 'Wq': Wq, 'bq': bq, 'Wk': Wk, 'bk': bk, 'Wv': Wv, 'bv': bv, 'Wg': Wg, 'bg': bg}
    _L1_attn_in = _L1_attn_setup()

    def _L1_ffn_setup():
        import jax, jax.numpy as jnp
        import numpy as np
        NUM_EXPERTS = 32
        TOP_K = 8
        SELECT_TOP_K = 4
        THRESHOLD = 0.5
        HIDDEN = 512
        D_FF = 192

        def _moe_forward(hidden_states, gate_weight, gate_up_proj, down_proj, similarity):
            B, S_len, H = hidden_states.shape
            E, K, Ssel = (NUM_EXPERTS, TOP_K, SELECT_TOP_K)
            x = hidden_states.reshape(-1, H)
            router_logits = x @ gate_weight.T
            router_probs = jax.nn.softmax(router_logits.astype(jnp.float32), axis=-1).astype(router_logits.dtype)
            router_top_value, router_indices = jax.lax.top_k(router_probs, K)
            routing_weights = router_top_value / jnp.clip(jnp.sum(router_top_value, axis=-1, keepdims=True), 1e-12, None)
            sim = similarity.astype(jnp.float32)
            sim = sim.at[jnp.arange(E), jnp.arange(E)].set(1.0)
            prim = router_indices[:, :Ssel]
            sec = router_indices[:, Ssel:]
            sim_cand = sim[sec[:, :, None], prim[:, None, :]]
            best_sim = jnp.max(sim_cand, axis=-1)
            best_i = jnp.argmax(sim_cand, axis=-1)
            prim_rep = jnp.broadcast_to(prim[:, None, :], sim_cand.shape)
            best_primary = jnp.take_along_axis(prim_rep, best_i[..., None], axis=-1)[..., 0]
            new_sec = jnp.where(best_sim < THRESHOLD, sec, best_primary) if THRESHOLD > 0.0 else best_primary
            rerouted_indices = jnp.concatenate([prim, new_sec], axis=1)
            combine = jnp.sum(jax.nn.one_hot(rerouted_indices, E, dtype=routing_weights.dtype) * routing_weights[..., None], axis=1)

            def expert_step(y, params):
                wgu, wd, cw = params
                gu = x @ wgu.T
                g, u = jnp.split(gu, 2, axis=-1)
                h = jax.nn.silu(g) * u
                y = y + h @ wd.T * cw[:, None]
                return (y, None)
            y0 = jnp.zeros_like(x)
            y, _ = jax.lax.scan(expert_step, y0, (gate_up_proj, down_proj, combine.T))
            return y.reshape(B, S_len, H)
        key = jax.random.key(seed)
        ks = jax.random.split(key, 5)
        hidden_states = jax.random.normal(ks[0], (4, 512, HIDDEN), dtype=jnp.float32)
        gate_weight = jax.random.normal(ks[1], (NUM_EXPERTS, HIDDEN), dtype=jnp.float32) * 0.02
        gate_up_proj = jax.random.normal(ks[2], (NUM_EXPERTS, 2 * D_FF, HIDDEN), dtype=jnp.float32) * 0.02
        down_proj = jax.random.normal(ks[3], (NUM_EXPERTS, HIDDEN, D_FF), dtype=jnp.float32) * 0.02
        similarity = jax.random.uniform(ks[4], (NUM_EXPERTS, NUM_EXPERTS), dtype=jnp.float32)
        return {'hidden_states': hidden_states, 'gate_weight': gate_weight, 'gate_up_proj': gate_up_proj, 'down_proj': down_proj, 'similarity': similarity}
    _L1_ffn_in = _L1_ffn_setup()
    _d = {'L0_attn_x': _L0_attn_in['x'], 'L0_attn_w_qkv': _L0_attn_in['w_qkv'], 'L0_attn_w_proj': _L0_attn_in['w_proj'], 'L0_attn_theta': _L0_attn_in['theta'], 'L0_ffn_w_gate': _L0_ffn_in['w_gate'], 'L0_ffn_w_up': _L0_ffn_in['w_up'], 'L0_ffn_w_down': _L0_ffn_in['w_down'], 'L0_ffn_s_gate': _L0_ffn_in['s_gate'], 'L0_ffn_s_up': _L0_ffn_in['s_up'], 'L0_ffn_s_down': _L0_ffn_in['s_down'], 'L1_attn_Wq': _L1_attn_in['Wq'], 'L1_attn_bq': _L1_attn_in['bq'], 'L1_attn_Wk': _L1_attn_in['Wk'], 'L1_attn_bk': _L1_attn_in['bk'], 'L1_attn_Wv': _L1_attn_in['Wv'], 'L1_attn_bv': _L1_attn_in['bv'], 'L1_attn_Wg': _L1_attn_in['Wg'], 'L1_attn_bg': _L1_attn_in['bg'], 'L1_ffn_gate_weight': _L1_ffn_in['gate_weight'], 'L1_ffn_gate_up_proj': _L1_ffn_in['gate_up_proj'], 'L1_ffn_down_proj': _L1_ffn_in['down_proj'], 'L1_ffn_similarity': _L1_ffn_in['similarity']}
    _x0 = _d['L0_attn_x']
    _d['L0_attn_x'] = jax.random.normal(jax.random.fold_in(jax.random.key(seed), 1), (4, 512, 512), dtype=_x0.dtype)
    del _x0
    return _d

def reference(L0_attn_x, L0_attn_w_qkv, L0_attn_w_proj, L0_attn_theta, L0_ffn_w_gate, L0_ffn_w_up, L0_ffn_w_down, L0_ffn_s_gate, L0_ffn_s_up, L0_ffn_s_down, L1_attn_Wq, L1_attn_bq, L1_attn_Wk, L1_attn_bk, L1_attn_Wv, L1_attn_bv, L1_attn_Wg, L1_attn_bg, L1_ffn_gate_weight, L1_ffn_gate_up_proj, L1_ffn_down_proj, L1_ffn_similarity):

    def _L0_attn_ref(x, w_qkv, w_proj, theta):
        import jax, jax.numpy as jnp
        import numpy as np
        DIM = 512
        HEADS = 16
        B = 4
        T = 512
        CHUNK = 128

        def _slopes(h):
            start = 2.0 ** (-2.0 ** (-(np.log2(h) - 3)))
            return np.array([start ** (i + 1) for i in range(h)], dtype=np.float32)

        def _lrpe(x, theta, offset=0):
            n = x.shape[-2]
            index = (jnp.arange(n, dtype=x.dtype) + offset).reshape(1, n, 1)
            th = theta * index
            return jnp.concatenate([x * jnp.cos(th), x * jnp.sin(th)], axis=-1)

        def _lightning_attn(q, k, v, slopes, chunk=CHUNK):
            b, h, Tn, dk = q.shape
            dv = v.shape[-1]
            nc = Tn // chunk
            s = slopes.reshape(h, 1, 1)
            idx = jnp.arange(chunk, dtype=q.dtype)
            diff = idx[:, None] - idx[None, :]
            diag_decay = jnp.where(diff >= 0, jnp.exp(-s * diff), 0.0)
            q_decay = jnp.exp(-s * (idx + 1.0)[None, :, None])
            k_decay = jnp.exp(-s * (chunk - 1.0 - idx)[None, :, None])
            block_decay = jnp.exp(-slopes * chunk).reshape(1, h, 1, 1)
            qc = q.reshape(b, h, nc, chunk, dk).transpose(2, 0, 1, 3, 4)
            kc = k.reshape(b, h, nc, chunk, dk).transpose(2, 0, 1, 3, 4)
            vc = v.reshape(b, h, nc, chunk, dv).transpose(2, 0, 1, 3, 4)

            def step(state, inp):
                qi, ki, vi = inp
                scores = jnp.einsum('bhid,bhjd->bhij', qi, ki) * diag_decay
                o = jnp.einsum('bhij,bhjv->bhiv', scores, vi) + jnp.einsum('bhid,bhdv->bhiv', qi * q_decay, state)
                state = block_decay * state + jnp.einsum('bhjd,bhjv->bhdv', ki * k_decay, vi)
                return (state, o)
            state0 = jnp.zeros((b, h, dk, dv), q.dtype)
            _, o = jax.lax.scan(step, state0, (qc, kc, vc))
            return o.transpose(1, 2, 0, 3, 4).reshape(b, h, Tn, dv)
        Bx, Tx, C = x.shape
        h = theta.shape[0]
        e = C // h
        qkv = x @ w_qkv.T
        q, k, v = jnp.split(qkv, 3, axis=-1)
        q = q.reshape(Bx, Tx, h, e).transpose(0, 2, 1, 3)
        k = k.reshape(Bx, Tx, h, e).transpose(0, 2, 1, 3)
        v = v.reshape(Bx, Tx, h, e).transpose(0, 2, 1, 3)
        q = _lrpe(q, theta, offset=0)
        k = _lrpe(k, theta, offset=0)
        slopes = jnp.asarray(_slopes(h))
        y = _lightning_attn(q, k, v, slopes)
        y = y.transpose(0, 2, 1, 3).reshape(Bx, Tx, C)
        return y @ w_proj.T

    def _L0_ffn_ref(x, w_gate, w_up, w_down, s_gate, s_up, s_down):
        import jax, jax.numpy as jnp
        import numpy as np
        HIDDEN = 512
        INTER = 2048
        B, S = (4, 256)

        def _qmatmul(x, w_int8, scale):
            y = jnp.einsum('bsh,ho->bso', x, w_int8.astype(x.dtype))
            return y * scale
        gate = jax.nn.silu(_qmatmul(x, w_gate, s_gate))
        up = _qmatmul(x, w_up, s_up)
        fuse = gate * up
        return _qmatmul(fuse, w_down, s_down)

    def _L1_attn_ref(x, Wq, bq, Wk, bk, Wv, bv, Wg, bg):
        import jax, jax.numpy as jnp
        import numpy as np
        DIM = 512
        q = jnp.einsum('bsd,ed->bse', x, Wq) + bq
        k = jnp.einsum('bsd,ed->bse', x, Wk) + bk
        v = jnp.einsum('bsd,ed->bse', x, Wv) + bv
        g = jax.nn.sigmoid(jnp.einsum('bsd,ed->bse', x, Wg) + bg)
        kv_state = jnp.cumsum(k * v, axis=1)
        return q * kv_state * g

    def _L1_ffn_ref(hidden_states, gate_weight, gate_up_proj, down_proj, similarity):
        import jax, jax.numpy as jnp
        import numpy as np
        NUM_EXPERTS = 32
        TOP_K = 8
        SELECT_TOP_K = 4
        THRESHOLD = 0.5
        HIDDEN = 512
        D_FF = 192

        def _moe_forward(hidden_states, gate_weight, gate_up_proj, down_proj, similarity):
            B, S_len, H = hidden_states.shape
            E, K, Ssel = (NUM_EXPERTS, TOP_K, SELECT_TOP_K)
            x = hidden_states.reshape(-1, H)
            router_logits = x @ gate_weight.T
            router_probs = jax.nn.softmax(router_logits.astype(jnp.float32), axis=-1).astype(router_logits.dtype)
            router_top_value, router_indices = jax.lax.top_k(router_probs, K)
            routing_weights = router_top_value / jnp.clip(jnp.sum(router_top_value, axis=-1, keepdims=True), 1e-12, None)
            sim = similarity.astype(jnp.float32)
            sim = sim.at[jnp.arange(E), jnp.arange(E)].set(1.0)
            prim = router_indices[:, :Ssel]
            sec = router_indices[:, Ssel:]
            sim_cand = sim[sec[:, :, None], prim[:, None, :]]
            best_sim = jnp.max(sim_cand, axis=-1)
            best_i = jnp.argmax(sim_cand, axis=-1)
            prim_rep = jnp.broadcast_to(prim[:, None, :], sim_cand.shape)
            best_primary = jnp.take_along_axis(prim_rep, best_i[..., None], axis=-1)[..., 0]
            new_sec = jnp.where(best_sim < THRESHOLD, sec, best_primary) if THRESHOLD > 0.0 else best_primary
            rerouted_indices = jnp.concatenate([prim, new_sec], axis=1)
            combine = jnp.sum(jax.nn.one_hot(rerouted_indices, E, dtype=routing_weights.dtype) * routing_weights[..., None], axis=1)

            def expert_step(y, params):
                wgu, wd, cw = params
                gu = x @ wgu.T
                g, u = jnp.split(gu, 2, axis=-1)
                h = jax.nn.silu(g) * u
                y = y + h @ wd.T * cw[:, None]
                return (y, None)
            y0 = jnp.zeros_like(x)
            y, _ = jax.lax.scan(expert_step, y0, (gate_up_proj, down_proj, combine.T))
            return y.reshape(B, S_len, H)
        return _moe_forward(hidden_states, gate_weight, gate_up_proj, down_proj, similarity)
    x = L0_attn_x
    x = _layernorm(x + _L0_attn_ref(x, L0_attn_w_qkv, L0_attn_w_proj, L0_attn_theta), axis=-1)
    x = _layernorm(x + _L0_ffn_ref(x, L0_ffn_w_gate, L0_ffn_w_up, L0_ffn_w_down, L0_ffn_s_gate, L0_ffn_s_up, L0_ffn_s_down), axis=-1)
    x = _layernorm(x + _L1_attn_ref(x, L1_attn_Wq, L1_attn_bq, L1_attn_Wk, L1_attn_bk, L1_attn_Wv, L1_attn_bv, L1_attn_Wg, L1_attn_bg), axis=-1)
    x = _layernorm(x + _L1_ffn_ref(x, L1_ffn_gate_weight, L1_ffn_gate_up_proj, L1_ffn_down_proj, L1_ffn_similarity), axis=-1)
    return x

_drawn_inputs = setup_inputs


def setup_inputs(seed=0):
    import zlib

    import numpy as np

    out = dict(_drawn_inputs(seed))
    spreads = {}
    factors = {'L1_attn_bg': 5.588,
     'L1_ffn_gate_weight': 3.799,
     'L1_ffn_gate_up_proj': 3.584,
     'L1_ffn_down_proj': 3.594,
     'L1_ffn_similarity': 8.0}
    for name, (base, spread) in spreads.items():
        noise = np.random.default_rng([zlib.crc32(name.encode()), seed]).standard_normal(out[name].shape)
        drawn = base * np.exp(spread * noise) if base else spread * noise
        out[name] = jnp.asarray(drawn.astype(out[name].dtype))
    for name, factor in factors.items():
        out[name] = (out[name] * factor).astype(out[name].dtype)
    return out
```

```python
from contextlib import ExitStack, contextmanager

import concourse.bass as bass
from concourse import mybir
from concourse.alu_op_type import AluOpType as ALU
import numpy as np

F32 = mybir.dt.float32
F16 = mybir.dt.float16
I8 = mybir.dt.int8
I32 = mybir.dt.int32
U32 = mybir.dt.uint32
ACT = mybir.ActivationFunctionType
AX = mybir.AxisListType.X

P = 128
DIM = 512
KD = DIM // P
BATCH, SEQ = 4, 512
TOK = BATCH * SEQ
NT = TOK // P
TB = SEQ // P
HEADS, HD = 16, 32
INTER = 2048
NM = INTER // P
EXPERTS, TOPK, PRIM, DFF = 32, 8, 4, 192
PAIRS = EXPERTS // 2
KT = 2 * DFF // P
WS = 16.0
FS = 64.0
EPS = 1e-5
MAGIC = 12582912.0
TWO_PI = (6.28125, float(np.float32(2 * np.pi - 6.28125)),
          float(2 * np.pi - 6.28125 - np.float64(np.float32(2 * np.pi - 6.28125))))
PI_MAX = 3.1415925


class Steps:

    def __init__(self, eng, sem):
        self.eng, self.sem, self.count, self.terms = eng, sem, 0, []

    def did(self, ins):
        ins.then_inc(self.sem, 1)
        self.count += 1

    def settle(self):
        v = self.count
        for i, per in self.terms:
            v = i * per + v
        self.eng.wait_ge(self.sem, v)

    @contextmanager
    def loop(self, lo, hi, per):
        base = self.count
        with self.eng.Fori(lo, hi) as i:
            self.terms.append((i, per))
            self.count = base - lo * per
            yield i
            assert self.count == base - lo * per + per, (self.count - base + lo * per, per)
            self.terms.pop()
        self.count = base + (hi - lo) * per


def build(nc, ins, out, stages=4):
    ctx = ExitStack()
    with ctx:
        def sb(name, shape, dt):
            return ctx.enter_context(nc.sbuf_tensor(name, shape, dt))

        def sem(name):
            return ctx.enter_context(nc.semaphore(name))

        X = sb("X", [P, NT, DIM], F32)
        XT = sb("XT", [P, 2, KD, TOK], F16)
        STG = sb("STG", [P, 6144], F32)
        WA = sb("WA", [P, 16384], F16)
        ARENA = sb("ARENA", [P, 22016], F32)
        ident16 = sb("ident16", [P, P], F16)
        ident32 = sb("ident32", [P, P], F32)
        mv = sb("mv", [P, TB, 2], F32)
        bs = sb("bs", [P, TB, 6], F32)
        rstd = sb("rstd", [P, TB, 2], F32)
        mhalf = sb("mhalf", [P, 2], F32)
        idle = sb("idle", [P, 1], F32)
        small = sb("small", [P, 144], F32)

        class Region:

            def __init__(self, buf, at=0):
                self.buf, self.at, self.unit = buf, at, 4 if buf.dtype == F32 else 2

            def take(self, shape, dt):
                n = int(np.prod(shape)) * {F32: 4, U32: 4, F16: 2, I8: 1}[dt]
                assert n % 4 == 0
                a = self.buf[:, self.at // self.unit:(self.at + n) // self.unit]
                self.at += n
                assert self.at <= self.buf.shape[1] * self.unit, self.at
                if dt != self.buf.dtype:
                    a = a.bitcast(dt)
                names = "abcd"[:len(shape)]
                kw = {names[i]: shape[i] for i in range(1, len(shape))}
                return a.rearrange(f"p ({' '.join(names)}) -> p {' '.join(names)}", **kw) if len(shape) > 1 else a

        r = Region(WA)
        Wqkv = r.take([2, KD, 3 * DIM], F16)
        Wproj = r.take([2, KD, DIM], F16)
        r = Region(ARENA)
        cosT, sinT = r.take([TB, DIM], F32), r.take([TB, DIM], F32)
        decT = r.take([HEADS, P], F32)
        qdec = r.take([KD, P], F32)
        QT = r.take([HEADS, 192], F16)
        KTk = r.take([HEADS, P], F16)
        qcs, kcs, kdecd = (r.take([HEADS, 64], F32) for _ in range(3))
        QA, QB, KA = (r.take([HEADS, P], F16) for _ in range(3))
        V = r.take([DIM], F32)
        Sd = r.take([HEADS, P], F32)
        state = r.take([HEADS, HD], F32)
        stateH, stateL = r.take([DIM], F16), r.take([DIM], F16)
        oT = r.take([KD, P], F32)
        oH, oL = r.take([KD, P], F16), r.take([KD, P], F16)
        resA = r.take([DIM], F32)
        hlA = r.take([2, DIM], F16)
        th, rr, kk = Sd[:, 0:4, :].rearrange("p a b -> p (a b)"), Sd[:, 4:8, :].rearrange("p a b -> p (a b)"), Sd[:, 8:12, :].rearrange("p a b -> p (a b)")
        theta = Sd[:, 12:16, :].rearrange("p a b -> p (a b)")
        kdec, decS, keep, nidx = small[:, 0:16], small[:, 16:32], small[:, 32:48], small[:, 48:52]
        r = Region(ARENA)
        Wg, Wu = r.take([KD, INTER], F16), r.take([KD, INTER], F16)
        Wd = r.take([NM, DIM], F16)
        sgB = r.take([2, DIM], F32)
        f32B = r.take([2, DIM], F32)
        fB = r.take([2, 2, DIM], F16)
        sdn = r.take([DIM], F32)
        resB = r.take([TB, DIM], F32)
        hlB = r.take([2, 2, DIM], F16)
        s_gateT, s_upT = small[:, 52:68], small[:, 68:84]
        raw8 = STG[:, :].bitcast(I8).rearrange("p (w n) -> p w n", w=12)
        raw8w = STG[:, :].bitcast(I32).rearrange("p (w n) -> p w n", w=12)
        Wc = Region(WA).take([2, KD, 4 * DIM], F16)
        r = Region(ARENA, 36864)
        kC, qC, gC, kvC, cumC, a1C, onesC = (r.take([SEQ], F32) for _ in range(7))
        aC = r.take([2, SEQ], F32)
        resC = r.take([TB, DIM], F32)
        hlC = r.take([2, 2, DIM], F16)
        biasC = small[:, 84:100]
        kb16, vb16 = small[:, 100:104], small[:, 104:108]
        r = Region(ARENA, 36864)
        oneh = r.take([NT, TOPK, EXPERTS], F32)
        prod = r.take([NT, TOPK, EXPERTS], F32)
        ohT = r.take([NT, P], F32)
        gwH = r.take([2, KD, EXPERTS], F16)
        bdsim = r.take([P], F32)
        iota = r.take([EXPERTS], F32)
        r = Region(WA)
        probs = r.take([NT, EXPERTS], F32)
        simrow = r.take([NT, PRIM, EXPERTS], F32)
        comb = r.take([NT, EXPERTS], F32)
        combT = r.take([TOK], F32)
        top8, idx, idxf, coef = r.take([NT, TOPK], F32), r.take([NT, TOPK], U32), r.take([NT, TOPK], F32), r.take([NT, TOPK], F32)
        cand, ind = r.take([NT, PRIM, PRIM], F32), r.take([NT, PRIM, PRIM], F32)
        best, rem, wmv, wtmp = (r.take([NT, PRIM], F32) for _ in range(4))
        mxr, smr = r.take([NT], F32), r.take([NT], F32)
        r = Region(ARENA)
        Wgu, Wdn = [], []
        for _ in range(2):
            Wgu.append(r.take([2, KD, 2 * 2 * DFF], F16))
            Wdn.append(r.take([2, KT, DIM], F16))
        cwb = [r.take([KT, TOK], F32) for _ in range(2)]
        r = Region(WA)
        sgD, aD = r.take([KT, DIM], F32), r.take([KT, DIM], F32)
        hD32 = r.take([KT, DIM], F32)
        hD = r.take([KT, 2, DIM], F16)
        outD = r.take([2, DIM], F32)
        rawgu = STG[:, 0:3072].rearrange("p (k n) -> p k n", k=KD)
        rawdn = STG[:, 3072:4608].rearrange("p (k n) -> p k n", k=KT)
        gwraw = STG[:, 4608:4608 + KD * EXPERTS].rearrange("p (k n) -> p k n", k=KD)

        cw_dram = nc.dram_tensor("cw_scratch", (EXPERTS, TOK), F32, kind="Internal").ap()

        bank = [ctx.enter_context(nc.psum_tensor(f"bank{i}", [P, 512], F32)) for i in range(8)]

        consts_in, x_in, w_split = sem("consts_in"), sem("x_in"), sem("w_split")
        w_raw = [sem(f"w_raw{i}") for i in range(4)]
        w_hi = sem("w_hi")
        tabs = sem("tabs")
        v_step, g_step, a_step = sem("v_step"), sem("g_step"), sem("a_step")
        setup = sem("setup")
        th_ready, sin_done = sem("th_ready"), sem("sin_done")
        q_ready, k_ready, v_proj, v_ready = sem("q_ready"), sem("k_ready"), sem("v_proj"), sem("v_ready")
        q_mul, k_mul, q_hi, k_hi, q_split, k_split, kdec_ready = (sem(n) for n in (
            "q_mul", "k_mul", "q_hi", "k_hi", "q_split", "k_split", "kdec_ready"))
        trans_ready, evac_act, evac_dve = sem("trans_ready"), sem("evac_act"), sem("evac_dve")
        s_ready, s_decayed, inter_ready, kv_ready = sem("s_ready"), sem("s_decayed"), sem("inter_ready"), sem("kv_ready")
        state_ready, state_hi, state_lo = sem("state_ready"), sem("state_hi"), sem("state_lo")
        pv_ready, o_ready, o_hi, o_lo, y_ready = sem("pv_ready"), sem("o_ready"), sem("o_hi"), sem("o_lo"), sem("y_ready")
        r_ready, ln_stat, ln_rstd, x_new, x_hi, x_lo, xt_trans, xt_new = (sem(n) for n in (
            "r_ready", "ln_stat", "ln_rstd", "x_new", "x_hi", "x_lo", "xt_trans", "xt_new"))
        b_raw, b_small, b_conv = sem("b_raw"), sem("b_small"), sem("b_conv")
        gate_ready, up_ready, silu_ready, f_ready, f_hi, f_lo, down_ready = (sem(n) for n in (
            "gate_ready", "up_ready", "silu_ready", "f_ready", "f_hi", "f_lo", "down_ready"))
        kc_ready, vc_ready, qc_ready, gc_ready, kc_sb, qc_sb, gc_sb, kvc, a1_ready, a_ready, at_ready = (sem(n) for n in (
            "kc_ready", "vc_ready", "qc_ready", "gc_ready", "kc_sb", "qc_sb", "gc_sb", "kvc", "a1_ready", "a_ready", "at_ready"))
        c_small = sem("c_small")
        logit_ready, exp_in, exp_out, oh_ready, ohT_ready, ohT_sb, simrow_ready, sim_used, comb_ready, combT_ready, combT_sb, cw_out = (sem(n) for n in (
            "logit_ready", "exp_in", "exp_out", "oh_ready", "ohT_ready", "ohT_sb", "simrow_ready", "sim_used", "comb_ready", "combT_ready", "combT_sb", "cw_out"))
        sim_in, r_small, bd_zero, bd_ready = sem("sim_in"), sem("r_small"), sem("bd_zero"), sem("bd_ready")
        p_raw, p_hi, p_split, cw_in = sem("p_raw"), sem("p_hi"), sem("p_split"), [sem("cw_in0"), sem("cw_in1")]
        g_ready, u_ready, sg_ready, aw_ready, h_ready, h_hi, h_lo, dn_ready, acc_done = (sem(n) for n in (
            "g_ready", "u_ready", "sg_ready", "aw_ready", "h_ready", "h_hi", "h_lo", "dn_ready", "acc_done"))
        out_ready, out_done = sem("out_ready"), sem("out_done")

        pieces = []
        for i in range(8):
            k, h = i // 2, i % 2
            pieces.append((ins["xT"][:, k, h * 1024:h * 1024 + 1024], 1.0, 1024,
                           XT[:, 0, k, h * 1024:h * 1024 + 1024], XT[:, 1, k, h * 1024:h * 1024 + 1024]))
        for k in range(KD):
            pieces.append((ins["wqkv"][:, k, :], WS, 1536, Wqkv[:, 0, k, :], Wqkv[:, 1, k, :]))
        for k in range(KD):
            pieces.append((ins["wproj"][:, k, :], WS, 512, Wproj[:, 0, k, :], Wproj[:, 1, k, :]))
        NPA = len(pieces)
        for k in range(KD):
            for h in range(2):
                pieces.append((ins["wc"][:, k, h * 1024:h * 1024 + 1024], WS, 1024,
                               Wc[:, 0, k, h * 1024:h * 1024 + 1024], Wc[:, 1, k, h * 1024:h * 1024 + 1024]))
        NPC = len(pieces)

        def slot(n):
            return STG[:, (n % 4) * 1536:(n % 4) * 1536 + pieces[n][2]]

        block = ctx.enter_context(nc.Block())

        @block.sync
        def _(sp):
            for dst, src in ((decT, ins["c_decT"]), (qdec, ins["c_qdec"]), (small[:, 0:52], ins["c_small"]),
                             (ident32[:, :], ins["c_ident32"]), (ident16[:, :], ins["c_ident16"]),
                             (theta, ins["theta"].partition_broadcast(P))):
                sp.dma_start(dst, src).then_inc(consts_in, 16)
            for n in range(NPA):
                if n >= 4:
                    sp.wait_ge(w_split, n - 3)
                sp.dma_start(slot(n), pieces[n][0]).then_inc(w_raw[n % 4], 16)
                if n == 11:
                    sp.dma_start(X[:, :, :], ins["x"]).then_inc(x_in, 16)
            if stages >= 2:
                sp.wait_ge(w_split, NPA)
                for w, name in enumerate(("w_gate", "w_up", "w_down")):
                    sp.dma_start(raw8w[:, 4 * w:4 * w + 4, :], ins[name]).then_inc(b_raw, 16)
                sp.dma_start(s_gateT, ins["s_gate"]).then_inc(b_small, 16)
                sp.dma_start(s_upT, ins["s_up"]).then_inc(b_small, 16)
                sp.wait_ge(y_ready, NT)
                sp.wait_ge(x_new, NT)
                sp.dma_start(sdn, ins["s_down"].partition_broadcast(P)).then_inc(b_small, 16)
            if stages >= 3:
                sp.wait_ge(b_conv, 12)
                for n in range(NPA, NPC):
                    if n >= NPA + 4:
                        sp.wait_ge(w_split, n - 3)
                    sp.dma_start(slot(n), pieces[n][0]).then_inc(w_raw[n % 4], 16)
                sp.dma_start(biasC, ins["bias_c"]).then_inc(c_small, 16)
            if stages >= 4:
                sp.wait_ge(w_split, NPC)
                sp.dma_start(rawgu, ins["wgu"][0]).then_inc(p_raw, 16)
                sp.dma_start(rawdn, ins["wdn"][0]).then_inc(p_raw, 16)
                sp.dma_start(gwraw, ins["gate_w"]).then_inc(r_small, 16)
                sp.wait_ge(x_new, 3 * NT)
                sp.wait_ge(xt_trans, 3 * NT)
                sp.dma_start(iota, ins["c_iota"]).then_inc(r_small, 16)
                sp.wait_ge(bd_zero, 1)
                for s in range(PRIM):
                    sp.dma_start(bdsim[32 * s:32 * s + 32, 32 * s:32 * s + 32], ins["sim"]).then_inc(sim_in, 16)
                sp.wait_ge(combT_sb, 4)
                sp.dma_start(cw_dram, combT[0:EXPERTS, :]).then_inc(cw_out, 16)
                sp.wait_ge(cw_out, 16)

                def combine_rows(p, par):
                    e0, e1 = (cw_dram[bass.ds(p * 2 + j, 1), :] for j in range(2))
                    for dst, src, n in ((cwb[par][:, 0, :], e0, P), (cwb[par][0:64, 1, :], e0, 64),
                                        (cwb[par][64:128, 1, :], e1, 64), (cwb[par][:, 2, :], e1, P)):
                        sp.dma_start(dst, src.to_broadcast([n, TOK])).then_inc(cw_in[par], 16)

                def next_weights(p):
                    sp.wait_ge(p_split, p * 4 + 4)
                    sp.dma_start(rawgu, ins["wgu"][bass.ds(p + 1, 1)].rearrange("a p k n -> p (a k) n")).then_inc(p_raw, 16)
                    sp.dma_start(rawdn, ins["wdn"][bass.ds(p + 1, 1)].rearrange("a p k n -> p (a k) n")).then_inc(p_raw, 16)

                combine_rows(0, 0)
                next_weights(0)
                combine_rows(1, 1)
                with sp.Fori(0, PAIRS // 2 - 1) as i:
                    for par in range(2):
                        next_weights(i * 2 + (par + 1))
                        sp.wait_ge(aw_ready, i * 24 + 12 * (par + 1))
                        combine_rows(i * 2 + (par + 2), par)
                for t in range(NT):
                    sp.wait_ge(out_ready, t + 1)
                    sp.dma_start(out[:, t, :], X[:, t, :]).then_inc(out_done, 16)
                sp.wait_ge(out_done, 16 * NT)
            else:
                sp.wait_ge(x_new, stages * NT)
                sp.wait_ge(xt_new, stages * NT)
                sp.dma_start(out, X[:, :, :]).then_inc(out_done, 16)
                sp.wait_ge(out_done, 16)

        def xt_transposes(pe, n, t, hl, dst):
            pe.wait_ge(x_lo, n + 1)
            d = dst[:, :].bitcast(F16)
            for j in range(2):
                for k in range(KD):
                    mm = pe.transpose(d[:, (j * KD + k) * P:(j * KD + k + 1) * P], hl[:, j, k * P:(k + 1) * P], ident16[:, :])
            mm.then_inc(xt_trans, 1)

        @block.tensor
        def _(pe):
            def three(dst, wa, wb, first=True, last=True):
                n = 0
                for a, b in ((0, 0), (0, 1), (1, 0)):
                    for k in range(KD):
                        mm = pe.matmul(dst, wa(a, k), wb(b, k), start=n == 0, stop=n == 3 * KD - 1)
                        n += 1
                return mm

            def proj(t, j, dst, done):
                tk = bass.ds(t * P, P)
                three(dst[:, :], lambda a, k: XT[:, a, k, tk], lambda b, k: Wqkv[:, b, k, j * DIM:(j + 1) * DIM]).then_inc(done, 1)

            pe.wait_ge(consts_in, 16 * 6)
            pe.wait_ge(w_split, 12)
            proj(0, 0, bank[0], q_ready)
            proj(0, 1, bank[1], k_ready)
            pe.wait_ge(q_mul, 1)
            proj(0, 2, bank[0], v_proj)
            pe.wait_ge(w_split, NPA)

            def attention(t, first, last):
                for g in range(6):
                    which, h0 = g % 3, 8 * (g // 3)
                    if g == 0:
                        pe.wait_ge(q_split, t + 1)
                    if g == 2:
                        pe.wait_ge(k_split, t + 1)
                    if g % 2 == 0:
                        pe.wait_ge(evac_act, t * 3 + g // 2)
                    else:
                        pe.wait_ge(evac_dve, t * 3 + g // 2)
                    d = bank[2 + g % 2][:, :].bitcast(F16)
                    for h in range(8):
                        src = (QT[:, h0 + h, 0:P], QT[:, h0 + h, 64:192], KTk[:, h0 + h, :])[which]
                        mm = pe.transpose(d[:, h * P:(h + 1) * P], src, ident16[:, :])
                    mm.then_inc(trans_ready, 1)
                for g in range(4):
                    if g == 0:
                        pe.wait_ge(evac_act, t * 3 + 2)
                        pe.wait_ge(evac_dve, t * 3 + 1)
                        pe.wait_ge(r_ready, t)
                    if g == 2:
                        pe.wait_ge(evac_act, t * 3 + 3)
                        pe.wait_ge(evac_dve, t * 3 + 3)
                    if g >= 2:
                        pe.wait_ge(s_decayed, t * 4 + g - 1)
                    for h in range(4 * g, 4 * g + 4):
                        d = bank[4 + g % 2][:, (h % 4) * P:(h % 4 + 1) * P]
                        pe.matmul(d, KA[:, h, :], QA[:, h, :], start=True, stop=False)
                        mm = pe.matmul(d, KA[:, h, :], QB[:, h, :], start=False, stop=True)
                    mm.then_inc(s_ready, 1)
                pe.wait_ge(state_lo, t + 1)
                pe.wait_ge(o_ready, t)
                for h in range(HEADS):
                    c, q = h // 4, 32 * (h % 4)
                    d = bank[6][q:q + 32, c * P:(c + 1) * P]
                    pe.matmul(d, stateH[:, h * HD:(h + 1) * HD], QA[:, h, :], start=True, stop=False)
                    mm = pe.matmul(d, stateL[:, h * HD:(h + 1) * HD], QA[:, h, :], start=False, stop=True)
                mm.then_inc(inter_ready, 1)
                pe.wait_ge(k_mul, t + 1)
                pe.wait_ge(kdec_ready, t + 1)
                pe.wait_ge(v_ready, t + 1)
                for h in range(HEADS):
                    for q in (0, 64):
                        mm = pe.matmul(bank[1][q:q + 64, h * HD:(h + 1) * HD], kdecd[:, h, :],
                                       V[:, h * HD:(h + 1) * HD], start=True, stop=True)
                mm.then_inc(kv_ready, 1)
                if not last:
                    proj(t + 1, 0, bank[0], q_ready)
                if not first:
                    pe.wait_ge(s_decayed, t * 4 + 4)
                    xt_transposes(pe, t - 1, t - 1, hlA, bank[5])
                if not last:
                    pe.wait_ge(state_ready, t + 1)
                    proj(t + 1, 1, bank[1], k_ready)
                pe.wait_ge(s_decayed, t * 4 + 4)
                for h in range(HEADS):
                    c, q = h // 4, 32 * (h % 4)
                    mm = pe.matmul(bank[7][q:q + 32, c * P:(c + 1) * P], V[:, h * HD:(h + 1) * HD], Sd[:, h, :],
                                   start=True, stop=True)
                mm.then_inc(pv_ready, 1)
                if not last:
                    pe.wait_ge(q_mul, t + 2)
                    proj(t + 1, 2, bank[0], v_proj)
                pe.wait_ge(o_lo, t + 1)
                o = (oH, oL)
                three(bank[4][:, :], lambda a, k: o[a][:, k, :], lambda b, k: Wproj[:, b, k, :]).then_inc(y_ready, 1)

            attention(0, True, False)
            with pe.Fori(1, NT - 1) as t:
                attention(t, False, False)
            attention(NT - 1, False, True)
            xt_transposes(pe, NT - 1, NT - 1, hlA, bank[5])

            def ffn(g, first):
                for m in range(NM):
                    s = g * NM + m
                    if m == 0:
                        pe.wait_ge(xt_new, g * TB + TB)
                        pe.wait_ge(b_conv, 12)
                    tk = bass.ds(g * SEQ, SEQ)
                    pe.wait_ge(silu_ready, s)
                    for n in range(2 * KD):
                        mm = pe.matmul(bank[0][:, :], Wg[:, n % KD, m * P:(m + 1) * P], XT[:, n // KD, n % KD, tk],
                                       start=n == 0, stop=n == 2 * KD - 1)
                    mm.then_inc(gate_ready, 1)
                    if not (first and m < 2):
                        pe.wait_ge(f_ready, s - 1)
                    for n in range(2 * KD):
                        mm = pe.matmul(bank[1 + m % 2][:, :], Wu[:, n % KD, m * P:(m + 1) * P], XT[:, n // KD, n % KD, tk],
                                       start=n == 0, stop=n == 2 * KD - 1)
                    mm.then_inc(up_ready, 1)
                    if m == 1:
                        pe.wait_ge(r_ready, g * TB + NT)
                    if m >= 1:
                        down(g, m - 1)
                    if not first and 7 <= m < 7 + TB:
                        n = g * TB + (NT - TB + m - 7)
                        pe.wait_ge(xt_new, n)
                        xt_transposes(pe, n, None, hlB[:, m % 2], bank[3])
                down(g, NM - 1)

            def down(g, m):
                pe.wait_ge(f_lo, g * NM + (m + 1))
                for tt in range(TB):
                    for a in range(2):
                        mm = pe.matmul(bank[4 + tt][:, :], fB[:, m % 2, a, tt * P:(tt + 1) * P], Wd[:, m, :],
                                       start=m == 0 and a == 0, stop=m == NM - 1 and a == 1)
                    if m == NM - 1:
                        mm.then_inc(down_ready, 1)

            if stages < 2:
                return
            pe.wait_ge(xt_new, NT)
            ffn(0, True)
            with pe.Fori(1, BATCH) as g:
                ffn(g, False)
            for tt in range(TB):
                pe.wait_ge(xt_new, 2 * NT - TB + tt)
                xt_transposes(pe, 2 * NT - TB + tt, None, hlB[:, (7 + tt) % 2], bank[3])
            if stages < 3:
                return

            order = ((1, kc_ready, 0), (2, vc_ready, 1), (0, qc_ready, 2), (3, gc_ready, 0))

            def back(g, et):
                s = g * KD + et
                pe.wait_ge(a_ready, s + 1)
                for tt in range(TB):
                    mm = pe.transpose(bank[4 + tt][:, et * P:(et + 1) * P], aC[:, et % 2, tt * P:(tt + 1) * P], ident32[:, :])
                mm.then_inc(at_ready, 1)

            def gated(g, first):
                tk = bass.ds(g * SEQ, SEQ)
                for et in range(KD):
                    s = g * KD + et
                    if et == 0:
                        pe.wait_ge(xt_new, g * TB + (NT + TB))
                    for j, done, b in order:
                        if j == 1:
                            pe.wait_ge(gc_sb, s)
                        if j == 2:
                            pe.wait_ge(kvc, s)
                        if j == 0:
                            pe.wait_ge(qc_sb, s)
                        if j == 3:
                            pe.wait_ge(kc_sb, s + 1)
                        three(bank[b][:, :], lambda a, k: Wc[:, a, k, j * DIM + et * P:j * DIM + (et + 1) * P],
                              lambda c, k: XT[:, c, k, tk]).then_inc(done, 1)
                        if j == 1 and et == 0 and not first:
                            back(g - 1, KD - 1)
                    if et == 1:
                        pe.wait_ge(r_ready, g * TB + 2 * NT)
                    if et >= 1:
                        back(g, et - 1)
                    if et == 3 and not first:
                        for tt in range(TB):
                            n = g * TB + (2 * NT - TB + tt)
                            pe.wait_ge(xt_new, n)
                            xt_transposes(pe, n, None, hlC[:, tt % 2], bank[3])

            pe.wait_ge(w_split, NPC)
            pe.wait_ge(xt_new, 2 * NT)
            gated(0, True)
            with pe.Fori(1, BATCH) as g:
                gated(g, False)
            back(BATCH - 1, KD - 1)
            for tt in range(TB):
                pe.wait_ge(xt_new, 3 * NT - TB + tt)
                xt_transposes(pe, 3 * NT - TB + tt, None, hlC[:, tt % 2], bank[3])
            if stages < 4:
                return

            pe.wait_ge(r_small, 16 * 2 + 1)
            pe.wait_ge(xt_new, 3 * NT)
            for t in range(NT):
                mm = three(bank[4][:, t * EXPERTS:(t + 1) * EXPERTS], lambda a, k: XT[:, a, k, t * P:(t + 1) * P],
                           lambda b, k: gwH[:, b, k, :])
            mm.then_inc(logit_ready, 1)
            pe.wait_ge(oh_ready, 1)
            for t in range(NT):
                b = bank[4 + t // 4]
                mm = pe.transpose(b[:, (t % 4) * P:(t % 4 + 1) * P],
                                  oneh[:, t, PRIM:TOPK, :].rearrange("p r e -> p (r e)"), ident32[:, :])
                if t % 4 == 3:
                    mm.then_inc(ohT_ready, 1)
            pe.wait_ge(bd_ready, 1)
            for t in range(NT):
                if t % 4 == 0:
                    pe.wait_ge(ohT_sb, t // 4 + 1)
                mm = pe.matmul(bank[4 + t // 4][:, (t % 4) * P:(t % 4 + 1) * P], ohT[:, t, :], bdsim[:, :], start=True, stop=True)
                if t % 4 == 3:
                    mm.then_inc(simrow_ready, 1)
            pe.wait_ge(comb_ready, 1)
            for t in range(NT):
                mm = pe.transpose(bank[4 + t // 4][0:EXPERTS, (t % 4) * P:(t % 4 + 1) * P], comb[:, t, :], ident32[:, :])
                if t % 4 == 3:
                    mm.then_inc(combT_ready, 1)

            def expert_down(p, tb, kt, par):
                s = p * 12 + (tb * 3 + kt)
                pe.wait_ge(h_lo, s + 1)
                for tt in range(TB):
                    for n, (a, b) in enumerate(((0, 0), (0, 1), (1, 0))):
                        mm = pe.matmul(bank[4 + tt][:, :], hD[:, kt, a, tt * P:(tt + 1) * P], Wdn[par][:, b, kt, :],
                                       start=kt == 0 and n == 0, stop=kt == KT - 1 and n == 2)
                if kt == KT - 1:
                    mm.then_inc(dn_ready, 1)

            def expert_block(p, tb, par, first, behind):
                tk = bass.ds(tb * SEQ, SEQ)
                for kt in range(KT):
                    s = p * 12 + (tb * 3 + kt)
                    pe.wait_ge(sg_ready, s)
                    three(bank[0][:, :], lambda a, k: Wgu[par][:, a, k, kt * P:(kt + 1) * P],
                          lambda b, k: XT[:, b, k, tk]).then_inc(g_ready, 1)
                    if not first:
                        pe.wait_ge(h_ready, s - 2)
                    three(bank[1 + kt][:, :], lambda a, k: Wgu[par][:, a, k, (KT + kt) * P:(KT + kt + 1) * P],
                          lambda b, k: XT[:, b, k, tk]).then_inc(u_ready, 1)
                    if kt == 0 and behind:
                        expert_down(behind[0], behind[1], KT - 1, behind[2])
                    if kt == 1:
                        pe.wait_ge(acc_done, p * 4 + tb)
                        if first:
                            pe.wait_ge(combT_sb, 4)
                    if kt >= 1:
                        expert_down(p, tb, kt - 1, par)

            def expert_pair(p, par, first=False):
                pe.wait_ge(p_split, p * 4 + 4)
                expert_block(p, 0, par, first, None if first else (p - 1, TB - 1, 1 - par))
                with pe.Fori(1, TB) as tb:
                    expert_block(p, tb, par, False, (p, tb - 1, par))

            expert_pair(0, 0, first=True)
            with pe.Fori(0, PAIRS // 2 - 1) as i:
                expert_pair(i * 2 + 1, 1)
                expert_pair(i * 2 + 2, 0)
            expert_pair(PAIRS - 1, 1)
            expert_down(PAIRS - 1, TB - 1, KT - 1, 1)

        @block.vector
        def _(dve):
            own = Steps(dve, v_step)

            def split_lo(src, scale, hi, lo):
                return dve.scalar_tensor_tensor(lo, src, scale, hi, ALU.mult, ALU.subtract)

            def ln_stats(res, slotn):
                own.did(dve.bn_stats(bs[:, slotn, :], res))
                own.settle()
                dve.memset(idle[:, :], 0.0)
                dve.bn_aggr(mv[:, slotn, :], bs[:, slotn, :]).then_inc(ln_stat, 1)

            def ln_apply(n, xt, res, slotn, done=x_new):
                dve.wait_ge(ln_stat, n + 1)
                dve.wait_ge(ln_rstd, n + 1)
                dve.tensor_scalar(xt, res, mv[:, slotn, 0:1], rstd[:, slotn, 1:2],
                                  ALU.subtract, ALU.mult).then_inc(done, 1)

            def tile(t):
                return X[:, bass.ds(t, 1), :].rearrange("p a n -> p (a n)")

            def split_piece(n):
                dve.wait_ge(w_hi, n + 1)
                src, scale, width, hi, lo = pieces[n]
                split_lo(slot(n), scale, hi, lo).then_inc(w_split, 1)

            for n in range(12):
                split_piece(n)
            dve.wait_ge(consts_in, 16 * 6)
            for c in range(TB):
                if c > 0:
                    dve.wait_ge(sin_done, 2 * c)
                own.did(dve.tensor_scalar(th, theta, nidx[:, c:c + 1], None, ALU.mult))
                own.settle()
                for j, (shift, dst) in enumerate(((0.0, sinT), (0.25, cosT))):
                    if j == 1:
                        dve.wait_ge(sin_done, 2 * c + 1)
                    own.did(dve.tensor_scalar(kk, th, 1 / (2 * np.pi), shift, ALU.mult, ALU.add))
                    own.settle()
                    own.did(dve.tensor_scalar(kk, kk, MAGIC, MAGIC, ALU.add, ALU.subtract))
                    own.settle()
                    own.did(dve.scalar_tensor_tensor(rr, kk, -TWO_PI[0], th, ALU.mult, ALU.add))
                    own.settle()
                    own.did(dve.scalar_tensor_tensor(rr, kk, -TWO_PI[1], rr, ALU.mult, ALU.add))
                    own.settle()
                    own.did(dve.scalar_tensor_tensor(rr, kk, -TWO_PI[2], rr, ALU.mult, ALU.add))
                    own.settle()
                    if j == 1:
                        own.did(dve.tensor_scalar(rr, rr, float(np.pi / 2), None, ALU.add))
                        own.settle()
                    dve.tensor_scalar(rr, rr, PI_MAX, -PI_MAX, ALU.min, ALU.max).then_inc(th_ready, 1)
            for n in range(12, NPA):
                split_piece(n)
            own.did(dve.memset(state, 0.0))
            own.did(dve.memset(stateH, 0.0))
            dve.memset(stateL, 0.0).then_inc(state_lo, 1)
            own.settle()
            dve.wait_ge(sin_done, 2 * TB)
            dve.wait_ge(x_in, 16)

            heads = lambda a: a.rearrange("p (h d) -> p h d", h=HEADS)

            def rotate(t, j):
                ready, free, dst, done = ((q_ready, q_split, qcs, q_mul), (k_ready, k_split, kcs, k_mul))[j]
                dve.wait_ge(ready, t + 1)
                if not isinstance(t, int) or t > 0:
                    dve.wait_ge(free, t)
                    if j == 1:
                        dve.wait_ge(kdec_ready, t)
                c = bass.ds(t % TB, 1)
                for n, tab in enumerate((cosT, sinT)):
                    i = dve.scalar_tensor_tensor(dst[:, :, n * HD:(n + 1) * HD], heads(bank[j][:, :]), 1 / WS,
                                                 heads(tab[:, c, :].rearrange("p a n -> p (a n)")), ALU.mult, ALU.mult)
                i.then_inc(done, 1)

            rotate(0, 0)
            rotate(0, 1)

            def attention(t, first, last):
                for g in (1, 3, 5):
                    dve.wait_ge(trans_ready, t * 6 + g + 1)
                    h0 = 8 * (g // 3)
                    dst = (QA, QB, KA)[g % 3]
                    dve.tensor_copy(dst[:, h0:h0 + 8, :].rearrange("p a b -> p (a b)"),
                                    bank[3][:, :].bitcast(F16)).then_inc(evac_dve, 1)
                if not first:
                    ln_apply(t - 1, tile(t - 1), resA, 0)
                for g in range(4):
                    dve.wait_ge(s_ready, t * 4 + g + 1)
                    i = dve.tensor_tensor(Sd[:, 4 * g:4 * g + 4, :].rearrange("p a b -> p (a b)"), bank[4 + g % 2][:, :],
                                          decT[:, 4 * g:4 * g + 4, :].rearrange("p a b -> p (a b)"), ALU.mult)
                    i.then_inc(s_decayed, 1)
                kp = keep[:, bass.ds(t, 1)]
                own.did(dve.scalar_tensor_tensor(state, state, kp, decS.unsqueeze(2).to_broadcast([P, HEADS, HD]), ALU.mult, ALU.mult))
                own.settle()
                dve.wait_ge(kv_ready, t + 1)
                st = state.rearrange("p h d -> p (h d)")
                dve.scalar_tensor_tensor(st, bank[1][:, :], kp, st, ALU.mult, ALU.add).then_inc(state_ready, 1)
                dve.wait_ge(state_hi, t + 1)
                dve.tensor_tensor(stateL, st, stateH, ALU.subtract).then_inc(state_lo, 1)
                if not last:
                    rotate(t + 1, 0)
                    rotate(t + 1, 1)
                ot = oT.rearrange("p a b -> p (a b)")
                dve.wait_ge(inter_ready, t + 1)
                own.did(dve.tensor_tensor(ot, bank[6][:, :], qdec.rearrange("p a b -> p (a b)"), ALU.mult))
                own.settle()
                dve.wait_ge(pv_ready, t + 1)
                dve.tensor_tensor(ot, ot, bank[7][:, :], ALU.add).then_inc(o_ready, 1)
                dve.wait_ge(o_hi, t + 1)
                dve.tensor_tensor(oL, oT, oH, ALU.subtract).then_inc(o_lo, 1)
                dve.wait_ge(y_ready, t + 1)
                dve.scalar_tensor_tensor(resA, bank[4][:, :], 1 / WS, tile(t), ALU.mult, ALU.add).then_inc(r_ready, 1)
                dve.wait_ge(r_ready, t + 1)
                ln_stats(resA, 0)

            attention(0, True, False)
            with own.loop(1, NT - 1, 3) as t:
                attention(t, False, False)
            attention(NT - 1, False, True)
            ln_apply(NT - 1, tile(NT - 1), resA, 0)

            if stages < 2:
                return
            dve.wait_ge(b_raw, 16 * 3)
            dve.wait_ge(xt_trans, NT)
            for w in range(0, 12, 3):
                dve.tensor_copy((Wg, Wu, Wd)[w // 4].rearrange("p a b -> p (a b)")[:, (w % 4) * 2048:(w % 4 + 1) * 2048],
                                raw8[:, w, :]).then_inc(b_conv, 1)
            dve.wait_ge(b_small, 16 * 3)
            own.did(dve.tensor_scalar(s_upT, s_upT, 1 / FS, None, ALU.mult))
            own.did(dve.tensor_scalar(sdn, sdn, FS, None, ALU.mult))
            own.settle()

            def ffn_residual(g):
                for tt in range(TB):
                    dve.wait_ge(down_ready, g * TB + (tt + 1))
                    own.did(dve.tensor_tensor(resB[:, tt, :], bank[4 + tt][:, :], sdn, ALU.mult))
                own.settle()
                for tt in range(TB):
                    dve.tensor_tensor(resB[:, tt, :], resB[:, tt, :], tile(g * TB + tt), ALU.add).then_inc(r_ready, 1)

            def ffn(g, first):
                n0 = g * TB + (NT - TB)
                for m in range(NM):
                    s = g * NM + m
                    dve.wait_ge(up_ready, s + 1)
                    dve.wait_ge(silu_ready, s + 1)
                    dve.scalar_tensor_tensor(f32B[:, m % 2, :], bank[1 + m % 2][:, :], s_upT[:, m:m + 1], sgB[:, m % 2, :],
                                             ALU.mult, ALU.mult).then_inc(f_ready, 1)
                    dve.wait_ge(f_hi, s + 1)
                    dve.tensor_tensor(fB[:, m % 2, 1, :], f32B[:, m % 2, :], fB[:, m % 2, 0, :], ALU.subtract).then_inc(f_lo, 1)
                    if not first and m < TB:
                        dve.wait_ge(r_ready, n0 + m + 1)
                        ln_stats(resB[:, m, :], m)
                    if not first and 1 <= m < TB + 1:
                        ln_apply(n0 + m - 1, tile(n0 + (m - 1 - NT)), resB[:, m - 1, :], m - 1)
                ffn_residual(g)

            ffn(0, True)
            with own.loop(1, BATCH, 2 * TB) as g:
                ffn(g, False)
            for tt in range(TB):
                dve.wait_ge(r_ready, 2 * NT - TB + tt + 1)
                ln_stats(resB[:, tt, :], tt)
            for tt in range(TB):
                ln_apply(2 * NT - TB + tt, tile(NT - TB + tt), resB[:, tt, :], tt)

            if stages < 3:
                return
            for n in range(NPA, NPC):
                split_piece(n)
            dve.wait_ge(c_small, 16)
            own.did(dve.memset(onesC, 1.0))
            own.did(dve.tensor_scalar(kb16, biasC[:, KD:2 * KD], 1 / WS, None, ALU.mult))
            own.did(dve.tensor_scalar(vb16, biasC[:, 2 * KD:3 * KD], WS, None, ALU.mult))
            own.settle()
            nop = dve.memset(bs[:, 0, 0:1], 0.0)
            nop.then_inc(c_small, 1)

            def gated(g, first):
                n0 = g * TB + (2 * NT - TB)
                for et in range(KD):
                    s = g * KD + et
                    dve.wait_ge(vc_ready, s + 1)
                    dve.wait_ge(kc_sb, s + 1)
                    dve.scalar_tensor_tensor(kvC, bank[1][:, :], vb16[:, et:et + 1], kC, ALU.add, ALU.mult).then_inc(kvc, 1)
                    dve.wait_ge(kvc, s + 1)
                    own.did(dve.tensor_tensor_scan(cumC, onesC, kvC, 0.0, ALU.mult, ALU.add))
                    own.settle()
                    dve.wait_ge(a1_ready, s + 1)
                    if not (first and et < 2):
                        dve.wait_ge(at_ready, s - 1)
                    dve.tensor_tensor(aC[:, et % 2, :], a1C, cumC, ALU.mult).then_inc(a_ready, 1)
                    if first:
                        continue
                    if et == 0:
                        dve.wait_ge(at_ready, s)
                        for tt in range(TB):
                            dve.tensor_tensor(resC[:, tt, :], bank[4 + tt][:, :], tile(n0 + (tt - 2 * NT)), ALU.add).then_inc(r_ready, 1)
                    if et == 1:
                        for tt in range(TB):
                            dve.wait_ge(r_ready, n0 + tt + 1)
                            ln_stats(resC[:, tt, :], tt)
                    if et == 2:
                        for tt in range(TB):
                            ln_apply(n0 + tt, tile(n0 + (tt - 2 * NT)), resC[:, tt, :], tt)

            gated(0, True)
            with own.loop(1, BATCH, KD + TB) as g:
                gated(g, False)
            dve.wait_ge(at_ready, BATCH * KD)
            n0 = 3 * NT - TB
            for tt in range(TB):
                dve.tensor_tensor(resC[:, tt, :], bank[4 + tt][:, :], tile(NT - TB + tt), ALU.add).then_inc(r_ready, 1)
                dve.wait_ge(r_ready, n0 + tt + 1)
                ln_stats(resC[:, tt, :], tt)
            for tt in range(TB):
                ln_apply(n0 + tt, tile(NT - TB + tt), resC[:, tt, :], tt)

            if stages < 4:
                return

            def pair_split(par, q, wait_n):
                dve.wait_ge(p_hi, wait_n)
                qs = bass.ds(q, 1)
                split_lo(rawgu[:, qs, :].rearrange("p a n -> p (a n)"), WS, Wgu[par][:, 0, qs, :].rearrange("p a n -> p (a n)"),
                         Wgu[par][:, 1, qs, :].rearrange("p a n -> p (a n)"))
                f = bass.ds(q * 384, 384)
                fl = lambda a: a.rearrange("p k n -> p (k n)")
                split_lo(fl(rawdn)[:, f], WS, fl(Wdn[par][:, 0])[:, f], fl(Wdn[par][:, 1])[:, f]).then_inc(p_split, 1)

            dve.wait_ge(p_raw, 32)
            for q in range(4):
                pair_split(0, q, q + 1)
            dve.wait_ge(r_small, 16 * 2)
            dve.wait_ge(w_hi, NPC + 1)
            split_lo(gwraw.rearrange("p k n -> p (k n)"), WS, gwH[:, 0].rearrange("p k n -> p (k n)"),
                     gwH[:, 1].rearrange("p k n -> p (k n)")).then_inc(r_small, 1)

            def step(ins_):
                own.did(ins_)
                own.settle()

            B3 = [P, NT, EXPERTS]
            dve.wait_ge(logit_ready, 1)
            L = bank[4][:, :].rearrange("p (t e) -> p t e", t=NT)
            step(dve.tensor_reduce(mxr, L, AX, ALU.max))
            dve.tensor_tensor(probs, L, mxr.unsqueeze(2).to_broadcast(B3), ALU.subtract).then_inc(exp_in, 1)
            dve.wait_ge(exp_out, 1)
            step(dve.tensor_reduce(smr, probs, AX, ALU.add))
            step(dve.reciprocal(smr, smr))
            step(dve.tensor_tensor(probs, probs, smr.unsqueeze(2).to_broadcast(B3), ALU.mult))
            for t in range(NT):
                own.did(dve.max(top8[:, t, :], probs[:, t, :]))
            own.settle()
            for t in range(NT):
                own.did(dve.max_index(idx[:, t, :], top8[:, t, :], probs[:, t, :]))
            own.settle()
            step(dve.tensor_copy(idxf, idx))
            rows = NT * TOPK
            dve.tensor_tensor(oneh.rearrange("p t r e -> p (t r) e"), iota.unsqueeze(1).to_broadcast([P, rows, EXPERTS]),
                              idxf.rearrange("p t r -> p (t r)").unsqueeze(2).to_broadcast([P, rows, EXPERTS]),
                              ALU.is_equal).then_inc(oh_ready, 1)
            dve.wait_ge(oh_ready, 1)
            step(dve.tensor_reduce(smr, top8, AX, ALU.add))
            step(dve.tensor_scalar(smr, smr, 1e-12, None, ALU.max))
            step(dve.reciprocal(smr, smr))
            step(dve.tensor_tensor(top8, top8, smr.unsqueeze(2).to_broadcast([P, NT, TOPK]), ALU.mult))
            for b in range(4):
                dve.wait_ge(ohT_ready, b + 1)
                dve.tensor_copy(ohT[:, 4 * b:4 * b + 4, :].rearrange("p a b -> p (a b)"), bank[4 + b][:, :]).then_inc(ohT_sb, 1)
            for b in range(4):
                dve.wait_ge(simrow_ready, b + 1)
                own.did(dve.tensor_copy(simrow[:, 4 * b:4 * b + 4].rearrange("p a b c -> p (a b c)"), bank[4 + b][:, :]))
            own.settle()
            for q in range(PRIM):
                pr = prod[:, :, 0:PRIM, :]
                step(dve.tensor_tensor(pr, simrow, oneh[:, :, q:q + 1, :].to_broadcast([P, NT, PRIM, EXPERTS]), ALU.mult))
                step(dve.tensor_reduce(cand[:, :, :, q], pr, AX, ALU.add))
            step(dve.tensor_reduce(best, cand, AX, ALU.max))
            step(dve.tensor_tensor(ind, cand, best.unsqueeze(3).to_broadcast([P, NT, PRIM, PRIM]), ALU.is_equal))
            step(dve.tensor_scalar(rem, ind[:, :, :, 0], -1.0, 1.0, ALU.mult, ALU.add))
            for q in range(1, PRIM):
                step(dve.tensor_tensor(ind[:, :, :, q], ind[:, :, :, q], rem, ALU.mult))
                if q < PRIM - 1:
                    step(dve.tensor_tensor(rem, rem, ind[:, :, :, q], ALU.subtract))
            step(dve.tensor_scalar(best, best, 0.5, None, ALU.is_lt))
            step(dve.tensor_tensor(coef[:, :, PRIM:TOPK], top8[:, :, PRIM:TOPK], best, ALU.mult))
            step(dve.tensor_tensor(wmv, top8[:, :, PRIM:TOPK], coef[:, :, PRIM:TOPK], ALU.subtract))
            step(dve.tensor_tensor(ind, ind, wmv.unsqueeze(3).to_broadcast([P, NT, PRIM, PRIM]), ALU.mult))
            step(dve.tensor_reduce(wtmp, ind.rearrange("p t s q -> p t q s"), AX, ALU.add))
            step(dve.tensor_tensor(coef[:, :, 0:PRIM], top8[:, :, 0:PRIM], wtmp, ALU.add))
            step(dve.tensor_tensor(prod.rearrange("p t r e -> p (t r) e"), oneh.rearrange("p t r e -> p (t r) e"),
                                   coef.rearrange("p t r -> p (t r)").unsqueeze(2).to_broadcast([P, rows, EXPERTS]), ALU.mult))
            dve.tensor_reduce(comb, prod.rearrange("p t r e -> p t e r"), AX, ALU.add).then_inc(comb_ready, 1)
            for b in range(4):
                dve.wait_ge(combT_ready, b + 1)
                dve.tensor_copy(combT[0:EXPERTS, b * 512:(b + 1) * 512], bank[4 + b][0:EXPERTS, :]).then_inc(combT_sb, 1)
            dve.wait_ge(cw_out, 16)

            def pair(p, par, last=False):
                def blk(tb):
                    for kt in range(KT):
                        s = p * 12 + (tb * 3 + kt)
                        dve.wait_ge(u_ready, s + 1)
                        dve.wait_ge(aw_ready, s + 1)
                        dve.tensor_tensor(hD32[:, kt, :], bank[1 + kt][:, :], aD[:, kt, :], ALU.mult).then_inc(h_ready, 1)
                        dve.wait_ge(h_hi, s + 1)
                        dve.tensor_tensor(hD[:, kt, 1, :], hD32[:, kt, :], hD[:, kt, 0, :], ALU.subtract).then_inc(h_lo, 1)
                        if kt == 1 and not last:
                            pair_split(1 - par, tb, p * 4 + tb + 5)
                        if kt == 1 and last and tb >= 1:
                            final_norm(tb - 1)
                    dve.wait_ge(dn_ready, p * 4 + tb + 1)
                    for tt in range(TB):
                        x = tile(tb * TB + tt)
                        i = dve.scalar_tensor_tensor(x, bank[4 + tt][:, :], 1 / (WS * WS), x, ALU.mult, ALU.add)
                    i.then_inc(acc_done, 1)
                    if last:
                        dve.wait_ge(acc_done, p * 4 + tb + 1)
                        for tt in range(TB):
                            ln_stats(X[:, tb * TB + tt, :], tt)

                def final_norm(tb):
                    for tt in range(TB):
                        x = X[:, tb * TB + tt, :]
                        ln_apply(3 * NT + tb * TB + tt, x, x, tt, out_ready)

                if last:
                    for tb in range(TB):
                        blk(tb)
                    final_norm(TB - 1)
                else:
                    with dve.Fori(0, TB) as tb:
                        blk(tb)

            pair(0, 0)
            with dve.Fori(0, PAIRS // 2 - 1) as i:
                pair(i * 2 + 1, 1)
                pair(i * 2 + 2, 0)
            pair(PAIRS - 1, 1, last=True)

        @block.scalar
        def _(act):
            def hi_piece(n):
                act.wait_ge(w_raw[n % 4], 16 * (n // 4 + 1))
                src, scale, width, hi, lo = pieces[n]
                act.activation(hi, slot(n), ACT.Copy, scale=scale).then_inc(w_hi, 1)

            def copy(dst, src, scale=1.0):
                return act.activation(dst, src, ACT.Copy, scale=scale)

            def tile(t):
                return X[:, bass.ds(t, 1), :].rearrange("p a n -> p (a n)")

            def xt_copy(n, t, src):
                act.wait_ge(xt_trans, n + 1)
                copy(XT[:, :, :, bass.ds(t * P, P)].rearrange("p a k n -> p (a k) n"),
                     src[:, :].bitcast(F16).rearrange("p (c n) -> p c n", c=2 * KD)).then_inc(xt_new, 1)

            for n in range(12):
                hi_piece(n)
            for c in range(TB):
                act.wait_ge(th_ready, 2 * c + 1)
                act.activation(sinT[:, c, :], rr, ACT.Sin).then_inc(sin_done, 1)
                act.wait_ge(th_ready, 2 * c + 2)
                act.activation(cosT[:, c, :], rr, ACT.Sin).then_inc(sin_done, 1)
            for n in range(12, NPA):
                hi_piece(n)

            def q_high(t):
                act.wait_ge(q_mul, t + 1)
                copy(QT[:, :, 0:64], qcs)
                copy(QT[:, :, 128:192], qcs).then_inc(q_hi, 1)

            def k_high(t):
                act.wait_ge(k_mul, t + 1)
                copy(KTk[:, :, 0:64], kcs).then_inc(k_hi, 1)

            def v_copy(t):
                act.wait_ge(v_proj, t + 1)
                copy(V, bank[0][:, :], 1 / WS).then_inc(v_ready, 1)

            q_high(0)
            k_high(0)
            v_copy(0)

            def attention(t, first, last):
                for g in (0, 2, 4):
                    act.wait_ge(trans_ready, t * 6 + g + 1)
                    h0 = 8 * (g // 3)
                    dst = (QA, QB, KA)[g % 3]
                    copy(dst[:, h0:h0 + 8, :].rearrange("p a b -> p (a b)"), bank[2][:, :].bitcast(F16)).then_inc(evac_act, 1)
                if not first:
                    act.wait_ge(x_new, t)
                    copy(hlA[:, 0, :], tile(t - 1)).then_inc(x_hi, 1)
                act.wait_ge(state_ready, t + 1)
                copy(stateH, state.rearrange("p h d -> p (h d)")).then_inc(state_hi, 1)
                if not first:
                    xt_copy(t - 1, t - 1, bank[5])
                if not last:
                    q_high(t + 1)
                    k_high(t + 1)
                act.wait_ge(o_ready, t + 1)
                copy(oH.rearrange("p a b -> p (a b)"), oT.rearrange("p a b -> p (a b)")).then_inc(o_hi, 1)
                if not last:
                    v_copy(t + 1)

            attention(0, True, False)
            with act.Fori(1, NT - 1) as t:
                attention(t, False, False)
            attention(NT - 1, False, True)
            act.wait_ge(x_new, NT)
            act.wait_ge(xt_trans, NT - 1)
            copy(hlA[:, 0, :], tile(NT - 1)).then_inc(x_hi, 1)
            xt_copy(NT - 1, NT - 1, bank[5])

            if stages < 2:
                return
            act.wait_ge(b_raw, 16 * 3)
            for w in [w for w in range(12) if w % 3 == 1]:
                copy((Wg, Wu, Wd)[w // 4].rearrange("p a b -> p (a b)")[:, (w % 4) * 2048:(w % 4 + 1) * 2048],
                     raw8[:, w, :]).then_inc(b_conv, 1)
            act.wait_ge(b_small, 16 * 3)

            def ffn(g, first):
                n0 = g * TB + (NT - TB)
                for m in range(NM):
                    s = g * NM + m
                    act.wait_ge(gate_ready, s + 1)
                    act.activation(sgB[:, m % 2, :], bank[0][:, :], ACT.Silu, scale=s_gateT[:, m:m + 1]).then_inc(silu_ready, 1)
                    act.wait_ge(f_ready, s + 1)
                    copy(fB[:, m % 2, 0, :], f32B[:, m % 2, :]).then_inc(f_hi, 1)
                    if not first and 5 <= m < 5 + TB:
                        tt = m - 5
                        act.wait_ge(x_new, n0 + tt + 1)
                        if tt >= 2:
                            act.wait_ge(xt_trans, n0 + tt - 1)
                        copy(hlB[:, m % 2, 0, :], tile(n0 + (tt - NT))).then_inc(x_hi, 1)
                    if not first and 7 <= m < 7 + TB:
                        xt_copy(n0 + (m - 7), n0 + (m - 7 - NT), bank[3])

            ffn(0, True)
            with act.Fori(1, BATCH) as g:
                ffn(g, False)

            def last_norms(base, hl, off):
                for tt in range(TB):
                    n = base + tt
                    act.wait_ge(x_new, n + 1)
                    if tt >= 2:
                        act.wait_ge(xt_trans, n - 1)
                    copy(hl[:, (off + tt) % 2, 0, :], tile(NT - TB + tt)).then_inc(x_hi, 1)
                    if tt >= 1:
                        xt_copy(n - 1, NT - TB + tt - 1, bank[3])
                xt_copy(base + TB - 1, NT - 1, bank[3])

            last_norms(2 * NT - TB, hlB, 1)

            if stages < 3:
                return
            for n in range(NPA, NPC):
                hi_piece(n)
            act.wait_ge(c_small, 17)

            def gated(g, first):
                n0 = g * TB + (2 * NT - TB)
                for et in range(KD):
                    s = g * KD + et
                    act.wait_ge(kc_ready, s + 1)
                    act.wait_ge(kvc, s)
                    act.activation(kC, bank[0][:, :], ACT.Identity, scale=1 / (WS * WS), bias=kb16[:, et:et + 1]).then_inc(kc_sb, 1)
                    act.wait_ge(qc_ready, s + 1)
                    act.wait_ge(a1_ready, s)
                    act.activation(qC, bank[2][:, :], ACT.Identity, scale=1 / WS, bias=biasC[:, et:et + 1]).then_inc(qc_sb, 1)
                    act.wait_ge(gc_ready, s + 1)
                    act.activation(gC, bank[0][:, :], ACT.Sigmoid, scale=1 / WS, bias=biasC[:, 3 * KD + et:3 * KD + et + 1]).then_inc(gc_sb, 1)
                    if et == 3 and not first:
                        for tt in range(TB):
                            n = n0 + tt
                            act.wait_ge(x_new, n + 1)
                            if tt >= 2:
                                act.wait_ge(xt_trans, n - 1)
                            copy(hlC[:, tt % 2, 0, :], tile(n0 + (tt - 2 * NT))).then_inc(x_hi, 1)
                            if tt >= 1:
                                xt_copy(n - 1, n0 + (tt - 1 - 2 * NT), bank[3])
                        xt_copy(n0 + 3, n0 + (3 - 2 * NT), bank[3])

            gated(0, True)
            with act.Fori(1, BATCH) as g:
                gated(g, False)
            last_norms(3 * NT - TB, hlC, 0)

            if stages < 4:
                return

            def pair_high(par, q):
                qs = bass.ds(q, 1)
                copy(Wgu[par][:, 0, qs, :].rearrange("p a n -> p (a n)"), rawgu[:, qs, :].rearrange("p a n -> p (a n)"), WS)
                f = bass.ds(q * 384, 384)
                fl = lambda a: a.rearrange("p k n -> p (k n)")
                copy(fl(Wdn[par][:, 0])[:, f], fl(rawdn)[:, f], WS).then_inc(p_hi, 1)

            act.wait_ge(p_raw, 32)
            for q in range(4):
                pair_high(0, q)
            act.wait_ge(r_small, 16 * 2)
            copy(gwH[:, 0].rearrange("p k n -> p (k n)"), gwraw.rearrange("p k n -> p (k n)"), WS).then_inc(w_hi, 1)
            act.wait_ge(exp_in, 1)
            pr = probs.rearrange("p t e -> p (t e)")
            act.activation(pr, pr, ACT.Exp, scale=1 / WS).then_inc(exp_out, 1)
            act.wait_ge(cw_out, 16)

            def pair(p, par, last=False):
                if not last:
                    act.wait_ge(p_raw, p * 32 + 64)
                with act.Fori(0, TB) as tb:
                    for kt in range(KT):
                        s = p * 12 + (tb * 3 + kt)
                        act.wait_ge(g_ready, s + 1)
                        act.activation(sgD[:, kt, :], bank[0][:, :], ACT.Silu, scale=1 / WS).then_inc(sg_ready, 1)
                        act.wait_ge(h_ready, s + 1)
                        copy(hD[:, kt, 0, :], hD32[:, kt, :]).then_inc(h_hi, 1)
                        if kt == 1 and not last:
                            act.wait_ge(dn_ready, p * 4)
                            pair_high(1 - par, tb)

            pair(0, 0)
            with act.Fori(0, PAIRS // 2 - 1) as i:
                pair(i * 2 + 1, 1)
                pair(i * 2 + 2, 0)
            pair(PAIRS - 1, 1, last=True)

        @block.gpsimd
        def _(pool):
            own = Steps(pool, g_step)

            def rstds(n, slotn):
                pool.wait_ge(ln_stat, n + 1)
                own.did(pool.tensor_tensor(rstd[:, slotn, 0:1], mv[:, slotn, 1:2], mhalf[:, 1:2], ALU.add))
                own.settle()
                pool.tensor_tensor(rstd[:, slotn, 1:2], rstd[:, slotn, 0:1], mhalf[:, 0:1], ALU.pow).then_inc(ln_rstd, 1)

            def tile(t):
                return X[:, bass.ds(t, 1), :].rearrange("p a n -> p (a n)")

            def x_low(n, t, hl):
                pool.wait_ge(x_hi, n + 1)
                pool.tensor_tensor(hl[:, 1, :], tile(t), hl[:, 0, :], ALU.subtract).then_inc(x_lo, 1)

            def q_low(t):
                pool.wait_ge(q_hi, t + 1)
                pool.tensor_tensor(QT[:, :, 64:128], qcs, QT[:, :, 0:64], ALU.subtract).then_inc(q_split, 1)

            def k_low(t):
                pool.wait_ge(k_hi, t + 1)
                pool.tensor_tensor(KTk[:, :, 64:128], kcs, KTk[:, :, 0:64], ALU.subtract).then_inc(k_split, 1)
                pool.tensor_tensor(kdecd, kcs, kdec.unsqueeze(2).to_broadcast([P, HEADS, 64]), ALU.mult).then_inc(kdec_ready, 1)

            own.did(pool.memset(mhalf[:, 0:1], -0.5))
            own.did(pool.memset(mhalf[:, 1:2], EPS))
            own.settle()
            pool.wait_ge(consts_in, 16 * 6)
            q_low(0)
            k_low(0)

            def attention(t, first, last):
                if not first:
                    rstds(t - 1, 0)
                    x_low(t - 1, t - 1, hlA)
                if not last:
                    q_low(t + 1)
                    k_low(t + 1)

            attention(0, True, False)
            with own.loop(1, NT - 1, 1) as t:
                attention(t, False, False)
            attention(NT - 1, False, True)
            rstds(NT - 1, 0)
            x_low(NT - 1, NT - 1, hlA)

            if stages < 2:
                return
            pool.wait_ge(b_raw, 16 * 3)
            pool.wait_ge(xt_trans, NT)
            for w in [w for w in range(12) if w % 3 == 2]:
                pool.tensor_copy((Wg, Wu, Wd)[w // 4].rearrange("p a b -> p (a b)")[:, (w % 4) * 2048:(w % 4 + 1) * 2048],
                                 raw8[:, w, :]).then_inc(b_conv, 1)

            def norms(n0, t0, hl, off):
                for tt in range(TB):
                    rstds(n0 + tt, tt)
                for tt in range(TB):
                    x_low(n0 + tt, t0 + tt, hl[:, (off + tt) % 2])

            with own.loop(0, BATCH, TB) as g:
                norms(g * TB + NT, g * TB, hlB, 1)

            if stages < 3:
                return
            def products(g, first):
                for et in range(KD):
                    s = g * KD + et
                    pool.wait_ge(gc_sb, s + 1)
                    pool.wait_ge(qc_sb, s + 1)
                    pool.wait_ge(a_ready, s)
                    pool.tensor_tensor(a1C, qC, gC, ALU.mult).then_inc(a1_ready, 1)
                    if first:
                        continue
                    n0 = g * TB + (2 * NT - TB)
                    if et == 1:
                        for tt in range(TB):
                            rstds(n0 + tt, tt)
                    if et == 3:
                        for tt in range(TB):
                            x_low(n0 + tt, n0 + (tt - 2 * NT), hlC[:, tt % 2])

            products(0, True)
            with own.loop(1, BATCH, TB) as g:
                products(g, False)
            norms(3 * NT - TB, NT - TB, hlC, 0)

            if stages < 4:
                return
            pool.wait_ge(x_new, 3 * NT)
            pool.wait_ge(xt_trans, 3 * NT)
            pool.memset(bdsim, 0.0).then_inc(bd_zero, 1)
            pool.wait_ge(sim_in, 16 * PRIM)
            pool.affine_select(out=bdsim, in_=bdsim, compare_op=ALU.not_equal, fill=1.0, base=0,
                               pattern=[[-1, P]], channel_multiplier=1).then_inc(bd_ready, 1)

            def pair(p, par, last=False):
                def blk(tb):
                    for kt in range(KT):
                        s = p * 12 + (tb * 3 + kt)
                        pool.wait_ge(cw_in[par], (p - par) * 32 + 64)
                        pool.wait_ge(sg_ready, s + 1)
                        pool.tensor_tensor(aD[:, kt, :], sgD[:, kt, :], cwb[par][:, kt, bass.ds(tb * SEQ, SEQ)],
                                           ALU.mult).then_inc(aw_ready, 1)
                        if kt == 1 and last and tb >= 1:
                            for tt in range(TB):
                                rstds(3 * NT + (tb - 1) * TB + tt, tt)

                if last:
                    for tb in range(TB):
                        blk(tb)
                    for tt in range(TB):
                        rstds(3 * NT + (TB - 1) * TB + tt, tt)
                else:
                    with pool.Fori(0, TB) as tb:
                        blk(tb)

            pair(0, 0)
            with pool.Fori(0, PAIRS // 2 - 1) as i:
                pair(i * 2 + 1, 1)
                pair(i * 2 + 2, 0)
            pair(PAIRS - 1, 1, last=True)


def _layouts(i):
    c = np.ascontiguousarray
    part = lambda a: c(a.reshape(a.shape[0] // P, P, -1).transpose(1, 0, 2))
    x = i["L0_attn_x"].reshape(TOK, DIM)
    d = {
        "x": part(x), "xT": part(x.T), "wqkv": part(i["L0_attn_w_qkv"].T), "wproj": part(i["L0_attn_w_proj"].T),
        "theta": c(i["L0_attn_theta"].reshape(DIM)),
        "w_gate": part(i["L0_ffn_w_gate"]).view(np.int32), "w_up": part(i["L0_ffn_w_up"]).view(np.int32),
        "w_down": part(i["L0_ffn_w_down"]).reshape(P, 4, 2048).view(np.int32),
        "s_gate": c(i["L0_ffn_s_gate"].reshape(NM, P).T), "s_up": c(i["L0_ffn_s_up"].reshape(NM, P).T),
        "s_down": c(i["L0_ffn_s_down"]),
        "wc": part(np.concatenate([i[f"L1_attn_W{n}"].T for n in "qkvg"], axis=1)),
        "bias_c": c(np.concatenate([i[f"L1_attn_b{n}"].reshape(KD, P).T for n in "qkvg"], axis=1)),
        "gate_w": part(i["L1_ffn_gate_weight"].T), "sim": c(i["L1_ffn_similarity"]),
    }
    gu = i["L1_ffn_gate_up_proj"].reshape(PAIRS, 2, 2, DFF, DIM)
    gu = gu.transpose(0, 2, 1, 3, 4).reshape(PAIRS, 4 * DFF, DIM)
    d["wgu"] = c(gu.transpose(0, 2, 1).reshape(PAIRS, KD, P, 4 * DFF).transpose(0, 2, 1, 3))
    dn = i["L1_ffn_down_proj"].transpose(0, 2, 1).reshape(PAIRS, KT, P, DIM)
    d["wdn"] = c(dn.transpose(0, 2, 1, 3))
    return d


def _constants():
    start = 2.0 ** (-2.0 ** (-(np.log2(HEADS) - 3)))
    s = np.array([start ** (n + 1) for n in range(HEADS)], dtype=np.float32)
    n = np.arange(P, dtype=np.float32)
    diff = n[None, :] - n[:, None]
    decT = np.where(diff[:, None, :] >= 0, np.exp(-s[None, :, None] * np.maximum(diff, 0)[:, None, :]), 0.0)
    head = (np.arange(KD)[None, :] * 4 + np.arange(P)[:, None] // HD)
    qdec = np.exp(-s[head][:, :, None] * (n + 1.0)[None, None, :])
    kdec = np.exp(-s[None, :] * (P - 1.0 - n)[:, None])
    decS = np.broadcast_to(np.exp(-s * P), (P, HEADS))
    keep = np.broadcast_to((np.arange(NT) % TB != TB - 1), (P, NT))
    nidx = n[:, None] + P * np.arange(TB)[None, :]
    f = lambda a: np.ascontiguousarray(a, dtype=np.float32)
    return {
        "c_decT": f(decT), "c_qdec": f(qdec), "c_small": f(np.concatenate([kdec, decS, keep, nidx], axis=1)),
        "c_ident32": f(np.eye(P)), "c_ident16": np.eye(P, dtype=np.float16),
        "c_iota": f(np.broadcast_to(np.arange(EXPERTS), (P, EXPERTS))),
    }


def kernel(**inputs):
    import concourse.bacc as bacc
    from concourse.bass_utils import run_bass_kernel_spmd as run

    arrays = {**_layouts({k: np.asarray(v) for k, v in inputs.items()}), **_constants()}
    nc = bacc.Bacc("TRN2", target_bir_lowering=False, num_devices=1)
    ins = {n: nc.dram_tensor(n, a.shape, mybir.dt.from_np(a.dtype), kind="ExternalInput").ap() for n, a in arrays.items()}
    out = nc.dram_tensor("out", (P, NT, DIM), F32, kind="ExternalOutput").ap()
    build(nc, ins, out)
    got = run(nc, [arrays], core_ids=[0]).results[0]["out"]
    return np.ascontiguousarray(got.transpose(1, 0, 2)).reshape(BATCH, SEQ, DIM)
```
